# Optimizing a Trainium2 kernel written in Bass

```python
import numpy as np
import jax
import jax.numpy as jnp

def _softmax(x, axis=-1):
    return jax.nn.softmax(x, axis=axis)

def _gelu(x):
    return jax.nn.gelu(x, approximate=True)

def _silu(x):
    return jax.nn.silu(x)

def _sigmoid(x):
    return jax.nn.sigmoid(x)

def _layernorm(x, axis=-1, eps=1e-05):
    m = jnp.mean(x, axis=axis, keepdims=True)
    v = jnp.var(x, axis=axis, keepdims=True)
    return (x - m) / jnp.sqrt(v + eps)

def _scatter_add(tgt, idx, src, axis=0):
    return tgt.at[idx].add(src)

def _segment_sum(src, seg, n):
    return jax.ops.segment_sum(src, seg, n)
kernel_name = 'mk_xattn_seq_d1_seqx_r8_c2124c'

def setup_inputs(seed: int=0):
    np.random.seed(seed)
    _w = jnp.asarray

    def _rec_inputs():
        import jax
        import jax.numpy as jnp
        _rk = jax.random.key(seed)
        x = 0.0002279 + 0.9999 * jax.random.normal(jax.random.fold_in(_rk, 1), (2, 256, 512), jnp.float32)
        _lenS = 256 - jax.random.randint(jax.random.fold_in(_rk, 7), (2,), 0, max(1, 256 // 4) + 1, jnp.int32)
        _lenS2 = 512 - jax.random.randint(jax.random.fold_in(_rk, 8), (2,), 0, max(1, 512 // 4) + 1, jnp.int32)
        _ctx_4096P = jax.random.normal(jax.random.fold_in(_rk, 11), (2, 16, 512), jnp.float32)
        _ctx_4096c = jax.random.dirichlet(jax.random.fold_in(_rk, 511), 0.3 * jnp.ones((16,), jnp.float32), (2, 512))
        _ctx_4096t = jnp.einsum('bsk,bkd->bsd', _ctx_4096c, _ctx_4096P)
        _ctx_4096t = _ctx_4096t * jax.lax.rsqrt(jnp.mean(jnp.square(_ctx_4096t)) + 1e-12) * 0.953939
        ctx_4096 = -0.000702761 + 1.00443 * (_ctx_4096t + 0.3 * jax.random.normal(jax.random.fold_in(_rk, 611), (2, 512, 512), jnp.float32))
        fside_BxSxS_0 = -0.000132966 + 0.0502041 * jax.random.normal(jax.random.fold_in(_rk, 12), (2, 256, 256), jnp.float32)
        return (x, ctx_4096, fside_BxSxS_0)
    x, ctx_4096, fside_BxSxS_0 = _rec_inputs()

    def _L0_xattn_setup():
        import jax, jax.numpy as jnp
        import numpy as np
        K = 8
        NUM_BLOCKS = 4
        SLOPE = 0.01

        def _lrelu(x):
            return jnp.where(x >= 0, x, SLOPE * x)

        def _knn_indices(xyz, k):
            sq = jnp.sum(xyz * xyz, axis=1)
            d2 = sq[:, :, None] + sq[:, None, :] - 2.0 * jnp.einsum('bdn,bdm->bnm', xyz, xyz)
            _, idx = jax.lax.top_k(-d2, k)
            return idx

        def _group_point(p, idx_t):
            return jnp.take_along_axis(p[:, :, None, :], idx_t, axis=3)
        key = jax.random.key(seed)
        k1, k2, k3, k4 = jax.random.split(key, 4)
        b, n, d = (4, 512, 64)
        xyz = jax.random.normal(k1, (b, 3, n), dtype=jnp.float32)
        points = jax.random.normal(k2, (b, d, n), dtype=jnp.float32)
        w_center = jax.random.normal(k3, (NUM_BLOCKS, d, d), dtype=jnp.float32) * 0.05
        w_neighbor = jax.random.normal(k4, (NUM_BLOCKS, d, d), dtype=jnp.float32) * 0.05
        return {'xyz': xyz, 'points': points, 'w_center': w_center, 'w_neighbor': w_neighbor}
    _L0_xattn_all = _L0_xattn_setup()
    _L0_xattn_in = {k: v for k, v in _L0_xattn_all.items() if k in ()}
    del _L0_xattn_all
    return {'x': x, 'ctx_4096': ctx_4096, 'fside_BxSxS_0': fside_BxSxS_0}

def reference(x, ctx_4096, fside_BxSxS_0):
    import jax
    import jax.numpy as jnp

    def _L0_xattn_ref(xyz, points, w_center, w_neighbor):
        import jax, jax.numpy as jnp
        import numpy as np
        K = 8
        NUM_BLOCKS = 4
        SLOPE = 0.01

        def _lrelu(x):
            return jnp.where(x >= 0, x, SLOPE * x)

        def _knn_indices(xyz, k):
            sq = jnp.sum(xyz * xyz, axis=1)
            d2 = sq[:, :, None] + sq[:, None, :] - 2.0 * jnp.einsum('bdn,bdm->bnm', xyz, xyz)
            _, idx = jax.lax.top_k(-d2, k)
            return idx

        def _group_point(p, idx_t):
            return jnp.take_along_axis(p[:, :, None, :], idx_t, axis=3)
        idx = _knn_indices(xyz, K)
        idx_t = jnp.transpose(idx, (0, 2, 1))[:, None, :, :]
        for i in range(NUM_BLOCKS):
            shortcut = points
            p = _lrelu(points)
            g = _group_point(p, idx_t)
            c = jnp.einsum('oi,bin->bon', w_center[i], p)
            gn = jnp.einsum('oi,bikn->bokn', w_neighbor[i], g)
            points = (c + gn.sum(axis=2)) / (K + 1.0) + shortcut
        return points
    x = _L0_xattn_ref(ctx_4096, x, fside_BxSxS_0, fside_BxSxS_0)
    return x

_drawn_inputs = setup_inputs


def setup_inputs(seed=0):
    import zlib

    import numpy as np

    out = dict(_drawn_inputs(seed))
    spreads = {}
    factors = {}
    for name, (base, spread) in spreads.items():
        noise = np.random.default_rng([zlib.crc32(name.encode()), seed]).standard_normal(out[name].shape)
        drawn = base * np.exp(spread * noise) if base else spread * noise
        out[name] = jnp.asarray(drawn.astype(out[name].dtype))
    for name, factor in factors.items():
        out[name] = (out[name] * factor).astype(out[name].dtype)
    return out
```

```python
import concourse.bass as bass
from concourse import mybir
from contextlib import ExitStack

FP32 = mybir.dt.float32
FP32R = mybir.dt.float32r
BF16 = mybir.dt.bfloat16
ALU = mybir.AluOpType
ACT = mybir.ActivationFunctionType


def knn_message_passing(nc, x_dram, ctx_dram, w_dram, out_dram):
    P = 128
    B, D, N = x_dram.shape
    C = ctx_dram.shape[1]
    NW = w_dram.shape[0]
    KNN = 8
    BLOCKS = 4
    SLOPE = 0.01
    CT, NT, DT = C // P, N // P, D // P
    H = 2
    TPB = NT // H
    TAKEN = -3.0e38
    assert NW == 2 and D * TPB == 512 and N == 512

    def made(block, per_block, more):
        j, c = block
        return j * per_block + (c * per_block + more)

    FIRST = (0, 0)

    ctx = ExitStack()
    with ctx:
        def sb(name, shape, dt=FP32):
            return ctx.enter_context(nc.sbuf_tensor(name, shape, dt))

        def sem(name):
            return ctx.enter_context(nc.semaphore(name))

        xyz = sb("xyz", [P, B, CT, N])
        xyz_head = sb("xyz_head", [P, B, CT, N], FP32R)
        xyz_tail = sb("xyz_tail", [P, B, CT, N], FP32R)
        rank = sb("rank", [P, B, NT, N])
        diag = sb("diag", [P, B, N])
        norms = sb("norms", [P, B, N])
        top = sb("top", [P, 2, KNN])
        left = sb("left", [P, 2, N])
        chosen = sb("chosen", [P, 2, N], BF16)
        mix = sb("mix", [P, B, NT, N], FP32R)
        feat = sb("feat", [P, B, DT, N])
        act = sb("act", [P, B, DT, N])
        act_head = sb("act_head", [P, B, DT, N], FP32R)
        act_tail = sb("act_tail", [P, B, DT, N], FP32R)
        w = sb("w", [P, NW, DT, D])
        wt_head = sb("wt_head", [P, NW, DT, D], FP32R)
        wt_tail = sb("wt_tail", [P, NW, DT, D], FP32R)
        t_head = sb("t_head", [P, B, NT, D], FP32R)
        t_tail = sb("t_tail", [P, B, NT, D], FP32R)
        ident = sb("ident", [P, P])
        ident_bf = sb("ident_bf", [P, P], BF16)
        halves = sb("halves", [P, P])

        bank = [ctx.enter_context(nc.psum_tensor(f"bank{i}", [P, 512], FP32)) for i in range(8)]
        gram = bank[0:4]
        u_ps = [bank[0:2], bank[2:4]]
        t_ps = [bank[4:6], bank[6:8]]
        wt_ps = bank[6:8]
        norms_ps = [bank[6], bank[2]]
        mixt_ps = [[bank[7], bank[6]], [bank[3], bank[2]]]

        xyz_loaded = [[sem(f"xyz_loaded{b}{c}") for c in range(CT)] for b in range(B)]
        x_loaded = [sem(f"x_loaded{b}") for b in range(B)]
        w_loaded = sem("w_loaded")
        out_stored = sem("out_stored")
        consts_ready = sem("consts_ready")
        const_step = sem("const_step")
        xyz_head_ready = sem("xyz_head_ready")
        xyz_tail_ready = sem("xyz_tail_ready")
        gram_done = sem("gram_done")
        upper_copied = sem("upper_copied")
        mirror_done = sem("mirror_done")
        lower_copied = sem("lower_copied")
        diag_ready = sem("diag_ready")
        norms_done = sem("norms_done")
        norms_copied = sem("norms_copied")
        rank_ready = sem("rank_ready")
        top_ready = sem("top_ready")
        left_ready = sem("left_ready")
        chosen_ready = sem("chosen_ready")
        mixt_done = sem("mixt_done")
        mix_ready = sem("mix_ready")
        wt_done = sem("wt_done")
        wt_head_ready = sem("wt_head_ready")
        wt_tail_ready = sem("wt_tail_ready")
        t_done = [sem(f"t_done{b}") for b in range(B)]
        t_head_ready = [sem(f"t_head_ready{b}") for b in range(B)]
        t_tail_ready = [sem(f"t_tail_ready{b}") for b in range(B)]
        u_done = [sem(f"u_done{b}") for b in range(B)]
        feat_ready = [sem(f"feat_ready{b}") for b in range(B)]
        act_ready = [sem(f"act_ready{b}") for b in range(B)]
        act_head_ready = [sem(f"act_head_ready{b}") for b in range(B)]
        act_tail_ready = [sem(f"act_tail_ready{b}") for b in range(B)]

        block = ctx.enter_context(nc.Block())

        @block.sync
        def _(sp):
            def load_xyz(b):
                for c in range(CT):
                    sp.dma_start(xyz[:, b, c, :], ctx_dram[b, c * P:(c + 1) * P, :]).then_inc(xyz_loaded[b][c], 16)

            def load_x(b):
                sp.dma_start(feat[:, b, :, :], x_dram[b].rearrange("(t p) n -> p t n", p=P)).then_inc(x_loaded[b], 16)

            load_xyz(0)
            sp.dma_start(w[:, :, :, :], w_dram.rearrange("k (t p) i -> p k t i", p=P)).then_inc(w_loaded, 16)
            load_x(0)
            load_xyz(1)
            load_x(1)
            for b in range(B):
                for t in range(DT):
                    sp.wait_ge(feat_ready[b], (BLOCKS - 1) * DT + t + 1)
                    sp.dma_start(out_dram[b, t * P:(t + 1) * P, :], feat[:, b, t, :]).then_inc(out_stored, 16)
            sp.wait_ge(out_stored, 16 * B * DT)

        @block.gpsimd
        def _(pool):
            pool.memset(halves[:, :], 0.5).then_inc(consts_ready, 1)
            pool.memset(ident[:, :], 0.0).then_inc(const_step, 1)
            pool.memset(ident_bf[:, :], 0.0).then_inc(const_step, 1)
            pool.wait_ge(const_step, 2)
            for m in (ident, ident_bf):
                pool.affine_select(out=m[:, :], in_=m[:, :], compare_op=ALU.not_equal, fill=1.0, base=0,
                                   pattern=[[-1, P]], channel_multiplier=1).then_inc(consts_ready, 1)

            def diagonal(b):
                for r in range(NT):
                    pool.wait_ge(upper_copied, b * NT + r + 1)
                    blk = slice(r * P, (r + 1) * P)
                    pool.affine_select(out=diag[:, b, blk], in_=rank[:, b, r, blk], compare_op=ALU.is_equal,
                                       fill=0.0, base=0, pattern=[[-1, P]],
                                       channel_multiplier=1).then_inc(diag_ready, 1)

            def ranks(b):
                pool.wait_ge(norms_copied, b + 1)
                for r in range(NT):
                    if r > 0:
                        pool.wait_ge(lower_copied, b * (NT - 1) + r)
                    pool.tensor_tensor(rank[:, b, r, :], rank[:, b, r, :], norms[:, b, :],
                                       ALU.subtract).then_inc(rank_ready, 1)

            def act_tails(b, k):
                for t in range(DT):
                    pool.wait_ge(act_head_ready[b], made(k, DT, t + 1))
                    pool.tensor_tensor(act_tail[:, b, t, :], act[:, b, t, :], act_head[:, b, t, :].bitcast(FP32),
                                       ALU.subtract).then_inc(act_tail_ready[b], 1)

            act_tails(0, FIRST)
            diagonal(0)
            ranks(0)
            act_tails(1, FIRST)
            diagonal(1)
            ranks(1)
            act_tails(0, (0, 1))
            with pool.Fori(0, BLOCKS - 1) as j:
                act_tails(1, (j, 1))
                act_tails(0, (j, 2))

        @block.scalar
        def _(se):
            def xyz_heads(b):
                for c in range(CT):
                    se.wait_ge(xyz_loaded[b][c], 16)
                    se.activation(xyz_head[:, b, c, :], xyz[:, b, c, :], ACT.Copy).then_inc(xyz_head_ready, 1)

            def wt_heads():
                for k in range(NW):
                    se.wait_ge(wt_done, k + 1)
                    se.activation(wt_head[:, k, :, :].rearrange("p t o -> p (t o)"), wt_ps[k][:, :],
                                  ACT.Copy).then_inc(wt_head_ready, 1)

            def upper(b):
                for r in range(NT):
                    se.wait_ge(gram_done, b * NT + r + 1)
                    se.activation(rank[:, b, r, r * P:N], gram[r][:, r * P:N], ACT.Copy,
                                  scale=2.0).then_inc(upper_copied, 1)

            def lower(b):
                for r in range(1, NT):
                    se.wait_ge(mirror_done, b * (NT - 1) + r)
                    se.activation(rank[:, b, r, 0:r * P], gram[r][:, 0:r * P], ACT.Copy).then_inc(lower_copied, 1)

            def norms_copy(b):
                se.wait_ge(norms_done, b + 1)
                se.activation(norms[:, b, :], norms_ps[b][:, :], ACT.Copy).then_inc(norms_copied, 1)

            def mix_copy(b, r):
                se.wait_ge(mixt_done, b * NT + r + 1)
                se.activation(mix[:, b, :, r * P:(r + 1) * P],
                              mixt_ps[b][r % 2][:, :].rearrange("p (m n) -> p m n", m=NT),
                              ACT.Copy).then_inc(mix_ready, 1)

            def t_heads(b, k):
                for h in range(H):
                    se.wait_ge(t_done[b], made(k, H, h + 1))
                    se.activation(t_head[:, b, h * TPB:(h + 1) * TPB, :].rearrange("p t o -> p (t o)"),
                                  t_ps[b][h][:, :], ACT.Copy).then_inc(t_head_ready[b], 1)

            def act_heads(b, k):
                for t in range(DT):
                    se.wait_ge(act_ready[b], made(k, DT, t + 1))
                    se.activation(act_head[:, b, t, :], act[:, b, t, :], ACT.Copy).then_inc(act_head_ready[b], 1)

            xyz_heads(0)
            act_heads(0, FIRST)
            wt_heads()
            xyz_heads(1)
            upper(0)
            lower(0)
            norms_copy(0)
            act_heads(1, FIRST)
            t_heads(0, FIRST)
            upper(1)
            mix_copy(0, 0)
            lower(1)
            mix_copy(0, 1)
            norms_copy(1)
            mix_copy(0, 2)
            mix_copy(0, 3)
            t_heads(1, FIRST)
            act_heads(0, (0, 1))
            for r in range(NT):
                mix_copy(1, r)
            with se.Fori(0, BLOCKS - 1) as j:
                t_heads(0, (j, 1))
                act_heads(1, (j, 1))
                act_heads(0, (j, 2))
                t_heads(1, (j, 1))

        @block.vector
        def _(ve):
            def xyz_tails(b):
                for c in range(CT):
                    ve.wait_ge(xyz_head_ready, b * CT + c + 1)
                    ve.tensor_tensor(xyz_tail[:, b, c, :], xyz[:, b, c, :], xyz_head[:, b, c, :].bitcast(FP32),
                                     ALU.subtract).then_inc(xyz_tail_ready, 1)

            def wt_tails():
                for k in range(NW):
                    ve.wait_ge(wt_head_ready, k + 1)
                    ve.tensor_tensor(wt_tail[:, k, :, :].rearrange("p t o -> p (t o)"), wt_ps[k][:, :],
                                     wt_head[:, k, :, :].rearrange("p t o -> p (t o)").bitcast(FP32),
                                     ALU.subtract).then_inc(wt_tail_ready, 1)

            def leaky(b, t):
                ve.scalar_tensor_tensor(act[:, b, t, :], feat[:, b, t, :], SLOPE, feat[:, b, t, :],
                                        ALU.mult, ALU.max).then_inc(act_ready[b], 1)

            def choose(b, r):
                n = b * NT + r
                ve.wait_ge(rank_ready, n + 1)
                ve.max(top[:, n % 2, :], rank[:, b, r, :]).then_inc(top_ready, 1)
                ve.wait_ge(top_ready, n + 1)
                ve.match_replace(left[:, n % 2, :], top[:, n % 2, :], rank[:, b, r, :],
                                 TAKEN).then_inc(left_ready, 1)
                ve.wait_ge(left_ready, n + 1)
                if n >= 2:
                    ve.wait_ge(mixt_done, n - 1)
                ve.tensor_scalar(chosen[:, n % 2, :], left[:, n % 2, :], TAKEN, None,
                                 ALU.is_equal).then_inc(chosen_ready, 1)

            def t_tails(b, k):
                for h in range(H):
                    ve.wait_ge(t_head_ready[b], made(k, H, h + 1))
                    ve.tensor_tensor(t_tail[:, b, h * TPB:(h + 1) * TPB, :].rearrange("p t o -> p (t o)"),
                                     t_ps[b][h][:, :],
                                     t_head[:, b, h * TPB:(h + 1) * TPB, :].rearrange("p t o -> p (t o)").bitcast(FP32),
                                     ALU.subtract).then_inc(t_tail_ready[b], 1)

            def update(b, k, t, last=False):
                ve.wait_ge(u_done[b], made(k, DT, t + 1))
                ve.scalar_tensor_tensor(feat[:, b, t, :], u_ps[b][t][:, :], 1.0 / (KNN + 1.0), feat[:, b, t, :],
                                        ALU.mult, ALU.add).then_inc(feat_ready[b], 1)
                if not last:
                    ve.wait_ge(feat_ready[b], made(k, DT, t + 1))
                    leaky(b, t)

            xyz_tails(0)
            ve.wait_ge(x_loaded[0], 16)
            for t in range(DT):
                leaky(0, t)
            wt_tails()
            xyz_tails(1)
            ve.wait_ge(x_loaded[1], 16)
            for t in range(DT):
                leaky(1, t)
            for r in range(NT):
                choose(0, r)
            t_tails(0, FIRST)
            choose(1, 0)
            choose(1, 1)
            update(0, FIRST, 0)
            choose(1, 2)
            update(0, FIRST, 1)
            choose(1, 3)
            t_tails(1, FIRST)
            with ve.Fori(0, BLOCKS - 1) as j:
                t_tails(0, (j, 1))
                for t in range(DT):
                    update(1, (j, 0), t)
                for t in range(DT):
                    update(0, (j, 1), t)
                t_tails(1, (j, 1))
            for t in range(DT):
                update(1, (0, BLOCKS - 1), t, last=True)

        @block.tensor
        def _(pe):
            def gram_tiles(b, c):
                pe.wait_ge(xyz_tail_ready, b * CT + c + 1)
                for r in range(NT):
                    if b > 0 and c == 0:
                        pe.wait_ge(upper_copied, (b - 1) * NT + r + 1)
                        if r > 0:
                            pe.wait_ge(lower_copied, (b - 1) * (NT - 1) + r)
                    rows = slice(r * P, (r + 1) * P)
                    parts = ((xyz_head, xyz_tail), (xyz_tail, xyz_head), (xyz_head, xyz_head))
                    for i, (left_part, right_part) in enumerate(parts):
                        mm = pe.matmul(gram[r][:, r * P:N], left_part[:, b, c, rows], right_part[:, b, c, r * P:N],
                                       start=(c == 0 and i == 0), stop=(c == CT - 1 and i == 2))
                    if c == CT - 1:
                        mm.then_inc(gram_done, 1)

            def mirror(b):
                for r in range(1, NT):
                    pe.wait_ge(upper_copied, b * NT + r + 1)
                    for q in range(r):
                        tr = pe.transpose(gram[r][:, q * P:(q + 1) * P], rank[:, b, q, r * P:(r + 1) * P],
                                          ident[:, :])
                    tr.then_inc(mirror_done, 1)

            def column_norms(b):
                pe.wait_ge(diag_ready, (b + 1) * NT)
                pe.matmul(norms_ps[b][:, :], halves[:, :], diag[:, b, :], start=True, stop=True).then_inc(norms_done, 1)

            def mix_tile(b, r):
                pe.wait_ge(chosen_ready, b * NT + r + 1)
                if r >= 2:
                    pe.wait_ge(mix_ready, b * NT + r - 1)
                out = mixt_ps[b][r % 2]
                n = (b * NT + r) % 2
                for m in range(NT):
                    mm = pe.matmul(out[:, m * P:(m + 1) * P], chosen[:, n, m * P:(m + 1) * P], ident_bf[:, :],
                                   start=True, stop=(m != r))
                    if m == r:
                        mm = pe.matmul(out[:, m * P:(m + 1) * P], ident_bf[:, :], ident_bf[:, :],
                                       start=False, stop=True)
                mm.then_inc(mixt_done, 1)

            def t_product(b, k, layer):
                pe.wait_ge(act_tail_ready[b], made(k, DT, DT))
                for h in range(H):
                    for j in range(TPB):
                        m = h * TPB + j
                        pts = slice(m * P, (m + 1) * P)
                        i = 0
                        for left_part, right_part in ((act_head, wt_tail), (act_head, wt_head), (act_tail, wt_head)):
                            for t in range(DT):
                                mm = pe.matmul(t_ps[b][h][:, j * D:(j + 1) * D], left_part[:, b, t, pts],
                                               right_part[:, layer, t, :], start=(i == 0), stop=(i == 3 * DT - 1))
                                i += 1
                    mm.then_inc(t_done[b], 1)

            def u_product(b, k):
                pe.wait_ge(t_tail_ready[b], made(k, H, H))
                for t in range(DT):
                    feats = slice(t * P, (t + 1) * P)
                    i = 0
                    for part in (t_tail, t_head):
                        for m in range(NT):
                            mm = pe.matmul(u_ps[b][t][:, :], part[:, b, m, feats], mix[:, b, m, :],
                                           start=(i == 0), stop=(i == 2 * NT - 1))
                            i += 1
                    mm.then_inc(u_done[b], 1)

            for c in range(CT):
                gram_tiles(0, c)
            pe.wait_ge(w_loaded, 16)
            pe.wait_ge(consts_ready, 3)
            for k in range(NW):
                for t in range(DT):
                    for o in range(DT):
                        tr = pe.transpose(wt_ps[k][:, t * D + o * P:t * D + (o + 1) * P], w[:, k, o, t * P:(t + 1) * P],
                                          ident[:, :])
                tr.then_inc(wt_done, 1)
            mirror(0)
            pe.wait_ge(wt_tail_ready, NW)
            column_norms(0)
            t_product(0, FIRST, 0)
            gram_tiles(1, 0)
            gram_tiles(1, 1)
            gram_tiles(1, 2)
            gram_tiles(1, 3)
            pe.wait_ge(norms_copied, 1)
            mix_tile(0, 0)
            mirror(1)
            mix_tile(0, 1)
            pe.wait_ge(lower_copied, 2 * (NT - 1))
            column_norms(1)
            mix_tile(0, 2)
            mix_tile(0, 3)
            pe.wait_ge(mix_ready, NT)
            u_product(0, FIRST)
            t_product(1, FIRST, 0)
            pe.wait_ge(norms_copied, 2)
            for r in range(NT):
                mix_tile(1, r)
            pe.wait_ge(mix_ready, 2 * NT)
            with pe.Fori(0, BLOCKS - 1) as j:
                t_product(0, (j, 1), 1)
                u_product(1, (j, 0))
                u_product(0, (j, 1))
                t_product(1, (j, 1), 1)
            u_product(1, (0, BLOCKS - 1))


def kernel(x, ctx_4096, fside_BxSxS_0):
    import numpy as np
    import concourse.bacc as bacc
    from concourse.bass_utils import run_bass_kernel_spmd

    nc = bacc.Bacc("TRN2", target_bir_lowering=False, num_devices=1)
    arrays, args = {}, []
    for name, a in (("x", x), ("ctx", ctx_4096), ("w", fside_BxSxS_0)):
        a = np.ascontiguousarray(a)
        arrays[f"{name}_dram"] = a
        args.append(nc.dram_tensor(f"{name}_dram", a.shape, mybir.dt.from_np(a.dtype), kind="ExternalInput").ap())
    args.append(nc.dram_tensor("out_dram", x.shape, FP32, kind="ExternalOutput").ap())
    knn_message_passing(nc, *args)
    r = run_bass_kernel_spmd(nc, [arrays], core_ids=[0])
    return r.results[0]["out_dram"]
```

```python
import concourse.bass as bass
from concourse import mybir
from contextlib import ExitStack

FP32 = mybir.dt.float32
FP32R = mybir.dt.float32r
BF16 = mybir.dt.bfloat16
ALU = mybir.AluOpType
ACT = mybir.ActivationFunctionType


def knn_message_passing(nc, x_dram, ctx_dram, wt_dram, out_dram):
    P = 128
    B, D, N = x_dram.shape
    C = ctx_dram.shape[1]
    NW = wt_dram.shape[0]
    KNN = 8
    BLOCKS = 4
    SLOPE = 0.01
    CT, NT, DT = C // P, N // P, D // P
    H = 2
    TPB = NT // H
    WARM = 9
    TAKEN = -3.0e38
    assert NW == 2 and D * TPB == 512 and N == 512

    def made(block, per_block, more):
        j, c = block
        return j * per_block + (c * per_block + more)

    FIRST, LAST = (0, 0), (0, BLOCKS - 1)

    ctx = ExitStack()
    with ctx:
        def sb(name, shape, dt=FP32):
            return ctx.enter_context(nc.sbuf_tensor(name, shape, dt))

        def sem(name):
            return ctx.enter_context(nc.semaphore(name))

        xyz = sb("xyz", [P, B, CT, N])
        xyz_head = sb("xyz_head", [P, B, CT, N], FP32R)
        xyz_tail = sb("xyz_tail", [P, B, CT, N], FP32R)
        gram2 = sb("gram2", [P, B, NT, N])
        rank = sb("rank", [P, B, NT, N])
        diag = sb("diag", [P, B, N])
        norms = sb("norms", [P, B, N])
        top = sb("top", [P, B * NT, KNN])
        left = sb("left", [P, 2, N])
        chosen = sb("chosen", [P, B * NT, N], BF16)
        mix = sb("mix", [P, B, NT, N], FP32R)
        feat = sb("feat", [P, B, DT, N])
        act = sb("act", [P, B, DT, N])
        act_head = sb("act_head", [P, B, DT, N], FP32R)
        act_tail = sb("act_tail", [P, B, DT, N], FP32R)
        wt = sb("wt", [P, NW, DT, D])
        wt_head = sb("wt_head", [P, NW, DT, D], FP32R)
        wt_tail = sb("wt_tail", [P, NW, DT, D], FP32R)
        t_head = sb("t_head", [P, B, NT, D], FP32R)
        t_tail = sb("t_tail", [P, B, NT, D], FP32R)
        ident = sb("ident", [P, P])
        ident_bf = sb("ident_bf", [P, P], BF16)
        halves = sb("halves", [P, P])
        zeros = sb("zeros", [P, N], BF16)

        bank = [ctx.enter_context(nc.psum_tensor(f"bank{i}", [P, 512], FP32)) for i in range(8)]
        gram = [bank[0:4], bank[4:8]]
        norms_ps = [bank[0], bank[4]]
        mixt_ps = [bank[2:4], bank[6:8]]
        t_ps = [bank[0:2], bank[2:4]]
        u_ps = [bank[4:6], bank[6:8]]

        PIECES = [[(t, slice(0, N), u_ps[b][t]) for t in range(DT)] for b in range(B)]
        PIECES[B - 1][DT - 1:] = [(DT - 1, slice(0, N // 2), u_ps[B - 1][DT - 1]),
                                  (DT - 1, slice(N // 2, N), t_ps[0][0])]

        xyz_loaded = [[sem(f"xyz_loaded{b}{c}") for c in range(CT)] for b in range(B)]
        x_loaded = [sem(f"x_loaded{b}") for b in range(B)]
        wt_loaded = sem("wt_loaded")
        out_stored = sem("out_stored")
        zeros_ready = sem("zeros_ready")
        consts_ready = sem("consts_ready")
        const_step = sem("const_step")
        xyz_head_ready = sem("xyz_head_ready")
        xyz_tail_ready = sem("xyz_tail_ready")
        gram_done = sem("gram_done")
        upper_copied = sem("upper_copied")
        mirror_done = sem("mirror_done")
        lower_copied = sem("lower_copied")
        diag_ready = sem("diag_ready")
        norms_done = sem("norms_done")
        norms_copied = sem("norms_copied")
        first_rank_ready = sem("first_rank_ready")
        rank_ready = sem("rank_ready")
        top_ready = sem("top_ready")
        left_ready = sem("left_ready")
        chosen_ready = sem("chosen_ready")
        mixt_done = sem("mixt_done")
        mix_ready = sem("mix_ready")
        wt_head_ready = sem("wt_head_ready")
        wt_tail_ready = sem("wt_tail_ready")
        t_done = [sem(f"t_done{b}") for b in range(B)]
        t_head_ready = [sem(f"t_head_ready{b}") for b in range(B)]
        t_tail_ready = [sem(f"t_tail_ready{b}") for b in range(B)]
        u_done = [sem(f"u_done{b}") for b in range(B)]
        feat_ready = [sem(f"feat_ready{b}") for b in range(B)]
        act_ready = [sem(f"act_ready{b}") for b in range(B)]
        act_head_ready = [sem(f"act_head_ready{b}") for b in range(B)]
        act_tail_ready = [sem(f"act_tail_ready{b}") for b in range(B)]

        block = ctx.enter_context(nc.Block())

        @block.sync
        def _(sp):
            def load_xyz(b):
                for c in range(CT):
                    sp.dma_start(xyz[:, b, c, :], ctx_dram[b, c * P:(c + 1) * P, :]).then_inc(xyz_loaded[b][c], 16)

            def load_x(b):
                sp.dma_start(feat[:, b, :, :], x_dram[b].rearrange("(t p) n -> p t n", p=P)).then_inc(x_loaded[b], 16)

            load_xyz(0)
            sp.dma_start(wt[:, :, :, :], wt_dram.rearrange("k (t p) o -> p k t o", p=P)).then_inc(wt_loaded, 16)
            load_x(0)
            load_xyz(1)
            load_x(1)
            for b in range(B):
                for i, (t, cols, _) in enumerate(PIECES[b]):
                    sp.wait_ge(feat_ready[b], made(LAST, DT, i + 1))
                    sp.dma_start(out_dram[b, t * P:(t + 1) * P, cols], feat[:, b, t, cols]).then_inc(out_stored, 16)
            sp.wait_ge(out_stored, 16 * sum(len(p) for p in PIECES))

        @block.gpsimd
        def _(pool):
            pool.memset(halves[:, :], 0.5).then_inc(consts_ready, 1)
            pool.memset(ident[:, :], 0.0).then_inc(const_step, 1)
            pool.memset(ident_bf[:, :], 0.0).then_inc(const_step, 1)
            pool.wait_ge(const_step, 2)
            for m in (ident, ident_bf):
                pool.affine_select(out=m[:, :], in_=m[:, :], compare_op=ALU.not_equal, fill=1.0, base=0,
                                   pattern=[[-1, P]], channel_multiplier=1).then_inc(consts_ready, 1)

            def diagonal(b):
                for r in range(NT):
                    pool.wait_ge(upper_copied, b * NT + r + 1)
                    blk = slice(r * P, (r + 1) * P)
                    pool.affine_select(out=diag[:, b, blk], in_=gram2[:, b, r, blk], compare_op=ALU.is_equal,
                                       fill=0.0, base=0, pattern=[[-1, P]],
                                       channel_multiplier=1).then_inc(diag_ready, 1)

            def ranks(b):
                pool.wait_ge(norms_copied, b + 1)
                for r in range(1, NT):
                    pool.wait_ge(lower_copied, b * (NT - 1) + r)
                    pool.tensor_tensor(rank[:, b, r, :], gram2[:, b, r, :], norms[:, b, :],
                                       ALU.subtract).then_inc(rank_ready, 1)

            def act_tails(b, k):
                for t in range(DT):
                    pool.wait_ge(act_head_ready[b], made(k, DT, t + 1))
                    pool.tensor_tensor(act_tail[:, b, t, :], act[:, b, t, :], act_head[:, b, t, :].bitcast(FP32),
                                       ALU.subtract).then_inc(act_tail_ready[b], 1)

            act_tails(0, FIRST)
            diagonal(0)
            act_tails(1, FIRST)
            ranks(0)
            diagonal(1)
            ranks(1)
            act_tails(0, (0, 1))
            act_tails(1, (0, 1))
            with pool.Fori(0, BLOCKS - 2) as j:
                act_tails(0, (j, 2))
                act_tails(1, (j, 2))

        @block.scalar
        def _(se):
            def xyz_heads(b):
                for c in range(CT):
                    se.wait_ge(xyz_loaded[b][c], 16)
                    se.activation(xyz_head[:, b, c, :], xyz[:, b, c, :], ACT.Copy).then_inc(xyz_head_ready, 1)

            def wt_heads():
                se.wait_ge(wt_loaded, 16)
                for k in range(NW):
                    se.activation(wt_head[:, k, :, :], wt[:, k, :, :], ACT.Copy).then_inc(wt_head_ready, 1)

            def upper(b):
                for r in range(NT):
                    se.wait_ge(gram_done, b * NT + r + 1)
                    se.activation(gram2[:, b, r, r * P:N], gram[b][r][:, r * P:N], ACT.Copy,
                                  scale=2.0).then_inc(upper_copied, 1)

            def lower(b):
                for r in range(1, NT):
                    se.wait_ge(mirror_done, b * (NT - 1) + r)
                    se.activation(gram2[:, b, r, 0:r * P], gram[b][r][:, 0:r * P], ACT.Copy).then_inc(lower_copied, 1)

            def norms_copy(b):
                se.wait_ge(norms_done, b + 1)
                se.activation(norms[:, b, :], norms_ps[b][:, :], ACT.Copy).then_inc(norms_copied, 1)

            def mix_copy(b, r):
                se.wait_ge(mixt_done, b * NT + r + 1)
                se.activation(mix[:, b, :, r * P:(r + 1) * P],
                              mixt_ps[b][r % 2][:, :].rearrange("p (m n) -> p m n", m=NT),
                              ACT.Copy).then_inc(mix_ready, 1)

            def t_heads(b, k):
                for h in range(H):
                    se.wait_ge(t_done[b], made(k, H, h + 1))
                    se.activation(t_head[:, b, h:NT:H, :], t_ps[b][h][:, :].rearrange("p (j o) -> p j o", j=TPB),
                                  ACT.Copy).then_inc(t_head_ready[b], 1)

            def act_heads(b, k):
                for t in range(DT):
                    se.wait_ge(act_ready[b], made(k, DT, t + 1))
                    se.activation(act_head[:, b, t, :], act[:, b, t, :], ACT.Copy).then_inc(act_head_ready[b], 1)

            xyz_heads(0)
            wt_heads()
            act_heads(0, FIRST)
            xyz_heads(1)
            upper(0)
            act_heads(1, FIRST)
            norms_copy(0)
            lower(0)
            mix_copy(0, 0)
            upper(1)
            mix_copy(0, 1)
            norms_copy(1)
            lower(1)
            mix_copy(0, 2)
            mix_copy(0, 3)
            t_heads(0, FIRST)
            t_heads(1, FIRST)
            for r in range(NT):
                mix_copy(1, r)
            act_heads(0, (0, 1))
            act_heads(1, (0, 1))
            with se.Fori(0, BLOCKS - 2) as j:
                t_heads(0, (j, 1))
                t_heads(1, (j, 1))
                act_heads(0, (j, 2))
                act_heads(1, (j, 2))
            t_heads(0, LAST)
            t_heads(1, LAST)

        @block.vector
        def _(ve):
            def xyz_tails(b):
                for c in range(CT):
                    ve.wait_ge(xyz_head_ready, b * CT + c + 1)
                    ve.tensor_tensor(xyz_tail[:, b, c, :], xyz[:, b, c, :], xyz_head[:, b, c, :].bitcast(FP32),
                                     ALU.subtract).then_inc(xyz_tail_ready, 1)

            def wt_tails():
                for k in range(NW):
                    ve.wait_ge(wt_head_ready, k + 1)
                    ve.tensor_tensor(wt_tail[:, k, :, :], wt[:, k, :, :], wt_head[:, k, :, :].bitcast(FP32),
                                     ALU.subtract).then_inc(wt_tail_ready, 1)

            def leaky(b, t):
                ve.scalar_tensor_tensor(act[:, b, t, :], feat[:, b, t, :], SLOPE, feat[:, b, t, :],
                                        ALU.mult, ALU.max).then_inc(act_ready[b], 1)

            def first_rank(b):
                ve.wait_ge(norms_copied, b + 1)
                ve.tensor_tensor(rank[:, b, 0, :], gram2[:, b, 0, :], norms[:, b, :],
                                 ALU.subtract).then_inc(first_rank_ready, 1)

            def find_top(n):
                b, r = n // NT, n % NT
                if r == 0:
                    ve.wait_ge(first_rank_ready, b + 1)
                else:
                    ve.wait_ge(rank_ready, b * (NT - 1) + r)
                ve.max(top[:, n, :], rank[:, n // NT, n % NT, :]).then_inc(top_ready, 1)

            def take_out(n):
                ve.wait_ge(top_ready, n + 1)
                ve.match_replace(left[:, n % 2, :], top[:, n, :], rank[:, n // NT, n % NT, :],
                                 TAKEN).then_inc(left_ready, 1)

            def mark(n):
                ve.wait_ge(left_ready, n + 1)
                ve.tensor_scalar(chosen[:, n, :], left[:, n % 2, :], TAKEN, None,
                                 ALU.is_equal).then_inc(chosen_ready, 1)

            def choose(n):
                find_top(n)
                if n % NT > 0:
                    mark(n - 1)
                take_out(n)
                if n % NT == NT - 1:
                    mark(n)

            def t_tails(b, k):
                for h in range(H):
                    ve.wait_ge(t_head_ready[b], made(k, H, h + 1))
                    ve.tensor_tensor(t_tail[:, b, h:NT:H, :], t_ps[b][h][:, :].rearrange("p (j o) -> p j o", j=TPB),
                                     t_head[:, b, h:NT:H, :].bitcast(FP32), ALU.subtract).then_inc(t_tail_ready[b], 1)

            def update(b, k):
                for t in range(DT):
                    ve.wait_ge(u_done[b], made(k, DT, t + 1))
                    ve.scalar_tensor_tensor(feat[:, b, t, :], u_ps[b][t][:, :], 1.0 / (KNN + 1.0), feat[:, b, t, :],
                                            ALU.mult, ALU.add).then_inc(feat_ready[b], 1)
                    ve.wait_ge(feat_ready[b], made(k, DT, t + 1))
                    leaky(b, t)

            def last_update(b, i):
                t, cols, ps = PIECES[b][i]
                ve.wait_ge(u_done[b], made(LAST, DT, i + 1))
                ve.scalar_tensor_tensor(feat[:, b, t, cols], ps[:, cols], 1.0 / (KNN + 1.0), feat[:, b, t, cols],
                                        ALU.mult, ALU.add).then_inc(feat_ready[b], 1)

            ve.memset(zeros[:, :], 0.0).then_inc(zeros_ready, 1)
            xyz_tails(0)
            ve.wait_ge(x_loaded[0], 16)
            for t in range(DT):
                leaky(0, t)
            wt_tails()
            xyz_tails(1)
            ve.wait_ge(x_loaded[1], 16)
            for t in range(DT):
                leaky(1, t)
            first_rank(0)
            for n in range(NT):
                choose(n)
            first_rank(1)
            choose(NT)
            choose(NT + 1)
            t_tails(0, FIRST)
            choose(NT + 2)
            choose(NT + 3)
            t_tails(1, FIRST)
            update(0, FIRST)
            update(1, FIRST)
            with ve.Fori(0, BLOCKS - 2) as j:
                t_tails(0, (j, 1))
                t_tails(1, (j, 1))
                update(0, (j, 1))
                update(1, (j, 1))
            t_tails(0, LAST)
            t_tails(1, LAST)
            for b in range(B):
                for i in range(len(PIECES[b])):
                    last_update(b, i)

        @block.tensor
        def _(pe):
            def gram_tile(b, c, r):
                rows = slice(r * P, (r + 1) * P)
                parts = ((xyz_head, xyz_tail), (xyz_tail, xyz_head), (xyz_head, xyz_head))
                for i, (left_part, right_part) in enumerate(parts):
                    mm = pe.matmul(gram[b][r][:, r * P:N], left_part[:, b, c, rows], right_part[:, b, c, r * P:N],
                                   start=(c == 0 and i == 0), stop=(c == CT - 1 and i == 2))
                if c == CT - 1:
                    mm.then_inc(gram_done, 1)

            def gram_tiles(b, c):
                pe.wait_ge(xyz_tail_ready, b * CT + c + 1)
                for r in range(NT):
                    gram_tile(b, c, r)

            def mirror(b):
                for r in range(1, NT):
                    pe.wait_ge(upper_copied, b * NT + r + 1)
                    for q in range(r):
                        tr = pe.transpose(gram[b][r][:, q * P:(q + 1) * P], gram2[:, b, q, r * P:(r + 1) * P],
                                          ident[:, :])
                    tr.then_inc(mirror_done, 1)

            def column_norms(b):
                pe.wait_ge(diag_ready, (b + 1) * NT)
                pe.matmul(norms_ps[b][:, :], halves[:, :], diag[:, b, :], start=True, stop=True).then_inc(norms_done, 1)

            def mix_tile(b, r):
                pe.wait_ge(chosen_ready, b * NT + r + 1)
                if r >= 2:
                    pe.wait_ge(mix_ready, b * NT + r - 1)
                out = mixt_ps[b][r % 2]
                n = b * NT + r
                for m in range(NT):
                    mm = pe.matmul(out[:, m * P:(m + 1) * P], chosen[:, n, m * P:(m + 1) * P], ident_bf[:, :],
                                   start=True, stop=(m != r))
                    if m == r:
                        mm = pe.matmul(out[:, m * P:(m + 1) * P], ident_bf[:, :], ident_bf[:, :],
                                       start=False, stop=True)
                mm.then_inc(mixt_done, 1)

            def t_product(b, k, layer):
                def products(m, parts, start, stop):
                    j = m // H
                    for i, (left_part, right_part, t) in enumerate(parts):
                        mm = pe.matmul(t_ps[b][m % H][:, j * D:(j + 1) * D], left_part[:, b, t, m * P:(m + 1) * P],
                                       right_part[:, layer, t, :], start=(start and i == 0),
                                       stop=(stop and i == len(parts) - 1))
                    return mm

                of_heads = [(act_head, part, t) for t in range(DT) for part in (wt_tail, wt_head)]
                of_tails = [(act_tail, wt_head, t) for t in range(DT)]
                pe.wait_ge(act_head_ready[b], made(k, DT, DT))
                for m in range(H):
                    products(m, of_heads, True, False)
                pe.wait_ge(act_tail_ready[b], made(k, DT, DT))
                for m in range(H):
                    products(m, of_tails, False, True)
                for m in range(H, NT):
                    products(m, of_heads + of_tails, True, True).then_inc(t_done[b], 1)

            def mixed(b, t, cols, ps):
                i = 0
                for part in (t_tail, t_head):
                    for m in range(NT):
                        mm = pe.matmul(ps[:, cols], part[:, b, m, t * P:(t + 1) * P], mix[:, b, m, cols],
                                       start=(i == 0), stop=(i == 2 * NT - 1))
                        i += 1
                mm.then_inc(u_done[b], 1)

            def u_product(b, k):
                pe.wait_ge(t_tail_ready[b], made(k, H, H))
                for t in range(DT):
                    mixed(b, t, slice(0, N), u_ps[b][t])

            pe.wait_ge(zeros_ready, 1)
            for i in range(WARM):
                pe.matmul(gram[1][3][:, :], zeros[:, 0:P], zeros[:, :], start=True, stop=True)
            for c in range(CT):
                gram_tiles(0, c)
            pe.wait_ge(xyz_tail_ready, CT + 1)
            gram_tile(1, 0, 0)
            gram_tile(1, 0, 1)
            pe.wait_ge(consts_ready, 3)
            column_norms(0)
            mirror(0)
            gram_tile(1, 0, 2)
            gram_tile(1, 0, 3)
            gram_tiles(1, 1)
            gram_tiles(1, 2)
            pe.wait_ge(lower_copied, NT - 1)
            mix_tile(0, 0)
            gram_tiles(1, 3)
            mix_tile(0, 1)
            column_norms(1)
            mirror(1)
            mix_tile(0, 2)
            pe.wait_ge(norms_copied, 1)
            pe.wait_ge(wt_tail_ready, NW)
            t_product(0, FIRST, 0)
            mix_tile(0, 3)
            pe.wait_ge(mix_ready, NT)
            t_product(1, FIRST, 0)
            pe.wait_ge(lower_copied, 2 * (NT - 1))
            mix_tile(1, 0)
            pe.wait_ge(norms_copied, 2)
            pe.wait_ge(t_tail_ready[0], H)
            mixed(0, 0, slice(0, N), u_ps[0][0])
            mix_tile(1, 1)
            mixed(0, 1, slice(0, N), u_ps[0][1])
            mix_tile(1, 2)
            mix_tile(1, 3)
            pe.wait_ge(mix_ready, 2 * NT)
            u_product(1, FIRST)
            with pe.Fori(0, BLOCKS - 2) as j:
                t_product(0, (j, 1), 1)
                t_product(1, (j, 1), 1)
                u_product(0, (j, 1))
                u_product(1, (j, 1))
            t_product(0, LAST, 1)
            t_product(1, LAST, 1)
            for b in range(B):
                pe.wait_ge(t_tail_ready[b], made(LAST, H, H))
                for piece in PIECES[b]:
                    mixed(b, *piece)


def kernel(x, ctx_4096, fside_BxSxS_0):
    import numpy as np
    import concourse.bacc as bacc
    from concourse.bass_utils import run_bass_kernel_spmd

    nc = bacc.Bacc("TRN2", target_bir_lowering=False, num_devices=1)
    arrays, args = {}, []
    wt = fside_BxSxS_0.transpose(0, 2, 1)
    for name, a in (("x", x), ("ctx", ctx_4096), ("wt", wt)):
        a = np.ascontiguousarray(a)
        arrays[f"{name}_dram"] = a
        args.append(nc.dram_tensor(f"{name}_dram", a.shape, mybir.dt.from_np(a.dtype), kind="ExternalInput").ap())
    args.append(nc.dram_tensor("out_dram", x.shape, FP32, kind="ExternalOutput").ap())
    knn_message_passing(nc, *args)
    r = run_bass_kernel_spmd(nc, [arrays], core_ids=[0])
    return r.results[0]["out_dram"]
```

```python
import concourse.bass as bass
from concourse import mybir
from contextlib import ExitStack

FP32 = mybir.dt.float32
FP32R = mybir.dt.float32r
BF16 = mybir.dt.bfloat16
ALU = mybir.AluOpType
ACT = mybir.ActivationFunctionType


def knn_message_passing(nc, x_dram, ctx_dram, wt_dram, out_dram):
    P = 128
    B, D, N = x_dram.shape
    C = ctx_dram.shape[1]
    NW = wt_dram.shape[0]
    KNN = 8
    BLOCKS = 4
    SLOPE = 0.01
    CT, NT, DT = C // P, N // P, D // P
    H = 2
    TPB = NT // H
    WARM = 7
    TAKEN = -3.0e38
    assert NW == 2 and D * TPB == 512 and N == 512

    def made(block, per_block, more):
        j, c = block
        return j * per_block + (c * per_block + more)

    FIRST, LAST = (0, 0), (0, BLOCKS - 1)

    ctx = ExitStack()
    with ctx:
        def sb(name, shape, dt=FP32):
            return ctx.enter_context(nc.sbuf_tensor(name, shape, dt))

        def sem(name):
            return ctx.enter_context(nc.semaphore(name))

        xyz = sb("xyz", [P, B, CT, N])
        xyz_head = sb("xyz_head", [P, B, CT, N], FP32R)
        xyz_tail = sb("xyz_tail", [P, B, CT, N], FP32R)
        gram2 = sb("gram2", [P, B, NT, N])
        rank = sb("rank", [P, B, NT, N])
        squares = sb("squares", [P, B, CT, N])
        norms = sb("norms", [P, B, N])
        top = sb("top", [P, B * NT, KNN])
        left = sb("left", [P, 2, N])
        chosen = sb("chosen", [P, B * NT, N], BF16)
        mix = sb("mix", [P, B, NT, N], FP32R)
        feat = sb("feat", [P, B, DT, N])
        act = sb("act", [P, B, DT, N])
        act_head = sb("act_head", [P, B, DT, N], FP32R)
        act_tail = sb("act_tail", [P, B, DT, N], FP32R)
        wt = sb("wt", [P, NW, DT, D])
        wt_head = sb("wt_head", [P, NW, DT, D], FP32R)
        wt_tail = sb("wt_tail", [P, NW, DT, D], FP32R)
        t_head = sb("t_head", [P, B, NT, D], FP32R)
        t_tail = sb("t_tail", [P, B, NT, D], FP32R)
        ident = sb("ident", [P, P])
        ident_bf = sb("ident_bf", [P, P], BF16)
        ones = sb("ones", [P, P])
        zeros = sb("zeros", [P, N], BF16)

        bank = [ctx.enter_context(nc.psum_tensor(f"bank{i}", [P, 512], FP32)) for i in range(8)]
        gram = [bank[0:4], bank[4:8]]
        norms_ps = [bank[7], bank[1]]
        mixt_ps = [bank[2:4], bank[6:8]]
        t_ps = [bank[0:2], bank[2:4]]
        u_ps = [bank[4:6], bank[6:8]]

        PIECES = [[(t, slice(0, N), u_ps[b][t]) for t in range(DT)] for b in range(B)]
        PIECES[B - 1][DT - 1:] = [(DT - 1, slice(0, N - P), u_ps[B - 1][DT - 1]),
                                  (DT - 1, slice(N - P, N), t_ps[0][0])]

        xyz_loaded = [[sem(f"xyz_loaded{b}{c}") for c in range(CT)] for b in range(B)]
        x_loaded = [sem(f"x_loaded{b}") for b in range(B)]
        wt_loaded = sem("wt_loaded")
        out_stored = sem("out_stored")
        zeros_ready = sem("zeros_ready")
        consts_ready = sem("consts_ready")
        const_step = sem("const_step")
        xyz_head_ready = sem("xyz_head_ready")
        xyz_tail_ready = sem("xyz_tail_ready")
        gram_done = sem("gram_done")
        upper_copied = sem("upper_copied")
        mirror_done = sem("mirror_done")
        lower_copied = sem("lower_copied")
        squares_ready = sem("squares_ready")
        pool_squares_ready = sem("pool_squares_ready")
        pairs_ready = sem("pairs_ready")
        square_sums_ready = sem("square_sums_ready")
        norms_done = sem("norms_done")
        norms_copied = sem("norms_copied")
        first_rank_ready = sem("first_rank_ready")
        rank_ready = sem("rank_ready")
        top_ready = sem("top_ready")
        left_ready = sem("left_ready")
        chosen_ready = sem("chosen_ready")
        mixt_done = sem("mixt_done")
        mix_ready = sem("mix_ready")
        wt_head_ready = sem("wt_head_ready")
        wt_tail_ready = sem("wt_tail_ready")
        t_done = [sem(f"t_done{b}") for b in range(B)]
        t_head_ready = [sem(f"t_head_ready{b}") for b in range(B)]
        t_tail_ready = [sem(f"t_tail_ready{b}") for b in range(B)]
        u_done = [sem(f"u_done{b}") for b in range(B)]
        feat_ready = [sem(f"feat_ready{b}") for b in range(B)]
        act_ready = [sem(f"act_ready{b}") for b in range(B)]
        act_head_ready = [sem(f"act_head_ready{b}") for b in range(B)]
        act_tail_ready = [[sem(f"act_tail_ready{b}{t}") for t in range(DT)] for b in range(B)]

        block = ctx.enter_context(nc.Block())

        @block.sync
        def _(sp):
            def load_xyz(b):
                for c in range(CT):
                    sp.dma_start(xyz[:, b, c, :], ctx_dram[b, c * P:(c + 1) * P, :]).then_inc(xyz_loaded[b][c], 16)

            def load_x(b):
                sp.dma_start(feat[:, b, :, :], x_dram[b].rearrange("(t p) n -> p t n", p=P)).then_inc(x_loaded[b], 16)

            load_xyz(0)
            sp.dma_start(wt[:, :, :, :], wt_dram.rearrange("k (t p) o -> p k t o", p=P)).then_inc(wt_loaded, 16)
            load_x(0)
            load_xyz(1)
            load_x(1)
            for b in range(B):
                for i, (t, cols, _) in enumerate(PIECES[b]):
                    sp.wait_ge(feat_ready[b], made(LAST, DT, i + 1))
                    sp.dma_start(out_dram[b, t * P:(t + 1) * P, cols], feat[:, b, t, cols]).then_inc(out_stored, 16)
            sp.wait_ge(out_stored, 16 * sum(len(p) for p in PIECES))

        @block.gpsimd
        def _(pool):
            pool.memset(ones[:, :], 1.0).then_inc(consts_ready, 1)
            pool.memset(ident[:, :], 0.0).then_inc(const_step, 1)
            pool.memset(ident_bf[:, :], 0.0).then_inc(const_step, 1)
            pool.wait_ge(const_step, 2)
            for m in (ident, ident_bf):
                pool.affine_select(out=m[:, :], in_=m[:, :], compare_op=ALU.not_equal, fill=1.0, base=0,
                                   pattern=[[-1, P]], channel_multiplier=1).then_inc(consts_ready, 1)

            def square(c):
                pool.wait_ge(xyz_loaded[0][c], 16)
                pool.tensor_tensor(squares[:, 0, c, :], xyz[:, 0, c, :], xyz[:, 0, c, :],
                                   ALU.mult).then_inc(pool_squares_ready, 1)

            def add_squares(b, c, d, out_ready):
                pool.tensor_tensor(squares[:, b, c, :], squares[:, b, c, :], squares[:, b, d, :],
                                   ALU.add).then_inc(out_ready, 1)

            def ranks(b):
                pool.wait_ge(norms_copied, b + 1)
                for r in range(1, NT):
                    pool.wait_ge(lower_copied, b * (NT - 1) + r)
                    pool.tensor_tensor(rank[:, b, r, :], gram2[:, b, r, :], norms[:, b, :],
                                       ALU.subtract).then_inc(rank_ready, 1)

            def act_tails(b, k, tiles=range(DT)):
                for t in tiles:
                    pool.wait_ge(act_head_ready[b], made(k, DT, t + 1))
                    pool.tensor_tensor(act_tail[:, b, t, :], act[:, b, t, :], act_head[:, b, t, :].bitcast(FP32),
                                       ALU.subtract).then_inc(act_tail_ready[b][t], 1)

            square(0)
            square(1)
            pool.wait_ge(pool_squares_ready, 2)
            add_squares(0, 0, 1, pairs_ready)
            pool.wait_ge(squares_ready, 2)
            add_squares(0, 2, 3, pairs_ready)
            pool.wait_ge(pairs_ready, 2)
            add_squares(0, 0, 2, square_sums_ready)
            act_tails(0, FIRST)
            ranks(0)
            pool.wait_ge(squares_ready, 2 + CT)
            add_squares(1, 0, 1, pairs_ready)
            add_squares(1, 2, 3, pairs_ready)
            act_tails(1, FIRST)
            ranks(1)
            act_tails(0, (0, 1))
            act_tails(1, (0, 1), [0])
            with pool.Fori(0, BLOCKS - 2) as j:
                act_tails(0, (j, 2))
                act_tails(1, (j, 2), [0])

        @block.scalar
        def _(se):
            def xyz_heads(b, tiles=range(CT)):
                for c in tiles:
                    se.wait_ge(xyz_loaded[b][c], 16)
                    se.activation(xyz_head[:, b, c, :], xyz[:, b, c, :], ACT.Copy).then_inc(xyz_head_ready, 1)

            def square(b, tiles=range(CT)):
                for c in tiles:
                    se.activation(squares[:, b, c, :], xyz[:, b, c, :], ACT.Square).then_inc(squares_ready, 1)

            def wt_heads():
                se.wait_ge(wt_loaded, 16)
                for k in range(NW):
                    se.activation(wt_head[:, k, :, :], wt[:, k, :, :], ACT.Copy).then_inc(wt_head_ready, 1)

            def upper(b, tiles=range(NT)):
                for r in tiles:
                    se.wait_ge(gram_done, b * NT + r + 1)
                    se.activation(gram2[:, b, r, r * P:N], gram[b][r][:, r * P:N], ACT.Copy,
                                  scale=2.0).then_inc(upper_copied, 1)

            def lower(b):
                for r in range(1, NT):
                    se.wait_ge(mirror_done, b * (NT - 1) + r)
                    se.activation(gram2[:, b, r, 0:r * P], gram[b][r][:, 0:r * P], ACT.Copy).then_inc(lower_copied, 1)

            def norms_copy(b):
                se.wait_ge(norms_done, b + 1)
                se.activation(norms[:, b, :], norms_ps[b][:, :], ACT.Copy).then_inc(norms_copied, 1)

            def mix_copy(b, r):
                se.wait_ge(mixt_done, b * NT + r + 1)
                se.activation(mix[:, b, :, r * P:(r + 1) * P],
                              mixt_ps[b][r % 2][:, :].rearrange("p (m n) -> p m n", m=NT),
                              ACT.Copy).then_inc(mix_ready, 1)

            def t_heads(b, k):
                for h in range(H):
                    se.wait_ge(t_done[b], made(k, H, h + 1))
                    se.activation(t_head[:, b, h:NT:H, :], t_ps[b][h][:, :].rearrange("p (j o) -> p j o", j=TPB),
                                  ACT.Copy).then_inc(t_head_ready[b], 1)

            def act_heads(b, k):
                for t in range(DT):
                    se.wait_ge(act_ready[b], made(k, DT, t + 1))
                    se.activation(act_head[:, b, t, :], act[:, b, t, :], ACT.Copy).then_inc(act_head_ready[b], 1)

            xyz_heads(0)
            square(0, [2, 3])
            wt_heads()
            act_heads(0, FIRST)
            xyz_heads(1)
            norms_copy(0)
            upper(0)
            lower(0)
            square(1)
            act_heads(1, FIRST)
            mix_copy(0, 0)
            mix_copy(0, 1)
            upper(1)
            norms_copy(1)
            lower(1)
            mix_copy(0, 2)
            mix_copy(0, 3)
            t_heads(0, FIRST)
            t_heads(1, FIRST)
            for r in range(NT):
                mix_copy(1, r)
            act_heads(0, (0, 1))
            act_heads(1, (0, 1))
            with se.Fori(0, BLOCKS - 2) as j:
                t_heads(0, (j, 1))
                t_heads(1, (j, 1))
                act_heads(0, (j, 2))
                act_heads(1, (j, 2))
            t_heads(0, LAST)
            t_heads(1, LAST)

        @block.vector
        def _(ve):
            def xyz_tails(b):
                for c in range(CT):
                    ve.wait_ge(xyz_head_ready, b * CT + c + 1)
                    ve.tensor_tensor(xyz_tail[:, b, c, :], xyz[:, b, c, :], xyz_head[:, b, c, :].bitcast(FP32),
                                     ALU.subtract).then_inc(xyz_tail_ready, 1)

            def wt_tails():
                for k in range(NW):
                    ve.wait_ge(wt_head_ready, k + 1)
                    ve.tensor_tensor(wt_tail[:, k, :, :], wt[:, k, :, :], wt_head[:, k, :, :].bitcast(FP32),
                                     ALU.subtract).then_inc(wt_tail_ready, 1)

            def leaky(b, t):
                ve.scalar_tensor_tensor(act[:, b, t, :], feat[:, b, t, :], SLOPE, feat[:, b, t, :],
                                        ALU.mult, ALU.max).then_inc(act_ready[b], 1)

            def first_rank(b):
                ve.wait_ge(norms_copied, b + 1)
                ve.wait_ge(upper_copied, b * NT + 1)
                ve.tensor_tensor(rank[:, b, 0, :], gram2[:, b, 0, :], norms[:, b, :],
                                 ALU.subtract).then_inc(first_rank_ready, 1)

            def find_top(n):
                b, r = n // NT, n % NT
                if r == 0:
                    ve.wait_ge(first_rank_ready, b + 1)
                else:
                    ve.wait_ge(rank_ready, b * (NT - 1) + r)
                ve.max(top[:, n, :], rank[:, n // NT, n % NT, :]).then_inc(top_ready, 1)

            def take_out(n):
                ve.wait_ge(top_ready, n + 1)
                ve.match_replace(left[:, n % 2, :], top[:, n, :], rank[:, n // NT, n % NT, :],
                                 TAKEN).then_inc(left_ready, 1)

            def mark(n):
                ve.wait_ge(left_ready, n + 1)
                ve.tensor_scalar(chosen[:, n, :], left[:, n % 2, :], TAKEN, None,
                                 ALU.is_equal).then_inc(chosen_ready, 1)

            def choose(n):
                find_top(n)
                if n % NT > 0:
                    mark(n - 1)
                take_out(n)
                if n == NT - 1:
                    ve.wait_ge(pairs_ready, 4)
                    ve.tensor_tensor(squares[:, 1, 0, :], squares[:, 1, 0, :], squares[:, 1, 2, :],
                                     ALU.add).then_inc(square_sums_ready, 1)
                if n % NT == NT - 1:
                    mark(n)

            def t_tails(b, k):
                for h in range(H):
                    ve.wait_ge(t_head_ready[b], made(k, H, h + 1))
                    ve.tensor_tensor(t_tail[:, b, h:NT:H, :], t_ps[b][h][:, :].rearrange("p (j o) -> p j o", j=TPB),
                                     t_head[:, b, h:NT:H, :].bitcast(FP32), ALU.subtract).then_inc(t_tail_ready[b], 1)

            def update(b, k):
                for t in range(DT):
                    ve.wait_ge(u_done[b], made(k, DT, t + 1))
                    ve.scalar_tensor_tensor(feat[:, b, t, :], u_ps[b][t][:, :], 1.0 / (KNN + 1.0), feat[:, b, t, :],
                                            ALU.mult, ALU.add).then_inc(feat_ready[b], 1)
                    ve.wait_ge(feat_ready[b], made(k, DT, t + 1))
                    leaky(b, t)

            def last_act_tail(k):
                b, t = B - 1, DT - 1
                ve.wait_ge(act_head_ready[b], made(k, DT, t + 1))
                ve.tensor_tensor(act_tail[:, b, t, :], act[:, b, t, :], act_head[:, b, t, :].bitcast(FP32),
                                 ALU.subtract).then_inc(act_tail_ready[b][t], 1)

            def last_update(b, i):
                t, cols, ps = PIECES[b][i]
                ve.wait_ge(u_done[b], made(LAST, DT, i + 1))
                ve.scalar_tensor_tensor(feat[:, b, t, cols], ps[:, cols], 1.0 / (KNN + 1.0), feat[:, b, t, cols],
                                        ALU.mult, ALU.add).then_inc(feat_ready[b], 1)

            ve.memset(zeros[:, :], 0.0).then_inc(zeros_ready, 1)
            xyz_tails(0)
            ve.wait_ge(x_loaded[0], 16)
            for t in range(DT):
                leaky(0, t)
            wt_tails()
            xyz_tails(1)
            first_rank(0)
            choose(0)
            ve.wait_ge(x_loaded[1], 16)
            for t in range(DT):
                leaky(1, t)
            for n in range(1, NT):
                choose(n)
            first_rank(1)
            choose(NT)
            choose(NT + 1)
            t_tails(0, FIRST)
            choose(NT + 2)
            choose(NT + 3)
            t_tails(1, FIRST)
            update(0, FIRST)
            update(1, FIRST)
            last_act_tail((0, 1))
            with ve.Fori(0, BLOCKS - 2) as j:
                t_tails(0, (j, 1))
                t_tails(1, (j, 1))
                update(0, (j, 1))
                update(1, (j, 1))
                last_act_tail((j, 2))
            t_tails(0, LAST)
            t_tails(1, LAST)
            for b in range(B):
                for i in range(len(PIECES[b])):
                    last_update(b, i)

        @block.tensor
        def _(pe):
            def gram_part(b, c, r, i):
                left_part, right_part = ((xyz_head, xyz_head), (xyz_head, xyz_tail), (xyz_tail, xyz_head))[i]
                mm = pe.matmul(gram[b][r][:, r * P:N], left_part[:, b, c, r * P:(r + 1) * P],
                               right_part[:, b, c, r * P:N], start=(c == 0 and i == 0), stop=(c == CT - 1 and i == 2))
                if c == CT - 1 and i == 2:
                    mm.then_inc(gram_done, 1)

            def gram_tiles(b, c, tiles=range(NT)):
                pe.wait_ge(xyz_tail_ready, b * CT + c + 1)
                for r in tiles:
                    for i in range(3):
                        gram_part(b, c, r, i)

            def mirror(b):
                for r in range(1, NT):
                    pe.wait_ge(upper_copied, b * NT + r + 1)
                    for q in range(r):
                        tr = pe.transpose(gram[b][r][:, q * P:(q + 1) * P], gram2[:, b, q, r * P:(r + 1) * P],
                                          ident[:, :])
                    tr.then_inc(mirror_done, 1)

            def column_norms(b):
                pe.wait_ge(square_sums_ready, b + 1)
                pe.matmul(norms_ps[b][:, :], ones[:, :], squares[:, b, 0, :], start=True,
                          stop=True).then_inc(norms_done, 1)

            def mix_tile(b, r):
                pe.wait_ge(chosen_ready, b * NT + r + 1)
                if r >= 2:
                    pe.wait_ge(mix_ready, b * NT + r - 1)
                out = mixt_ps[b][r % 2]
                n = b * NT + r
                for m in range(NT):
                    mm = pe.matmul(out[:, m * P:(m + 1) * P], chosen[:, n, m * P:(m + 1) * P], ident_bf[:, :],
                                   start=True, stop=(m != r))
                    if m == r:
                        mm = pe.matmul(out[:, m * P:(m + 1) * P], ident_bf[:, :], ident_bf[:, :],
                                       start=False, stop=True)
                mm.then_inc(mixt_done, 1)

            def t_product(b, k, layer):
                def products(m, parts, start, stop):
                    j = m // H
                    for i, (left_part, right_part, t) in enumerate(parts):
                        mm = pe.matmul(t_ps[b][m % H][:, j * D:(j + 1) * D], left_part[:, b, t, m * P:(m + 1) * P],
                                       right_part[:, layer, t, :], start=(start and i == 0),
                                       stop=(stop and i == len(parts) - 1))
                    return mm

                of_heads = [(act_head, part, t) for t in range(DT) for part in (wt_tail, wt_head)]
                of_tails = [(act_tail, wt_head, t) for t in range(DT)]
                pe.wait_ge(act_head_ready[b], made(k, DT, DT))
                for m in range(H):
                    products(m, of_heads, True, False)
                for t in range(DT):
                    pe.wait_ge(act_tail_ready[b][t], made(k, 1, 1))
                for m in range(H):
                    products(m, of_tails, False, True)
                for m in range(H, NT):
                    products(m, of_heads + of_tails, True, True).then_inc(t_done[b], 1)

            def mixed_part(b, t, cols, ps, i):
                part = (t_tail, t_head)[i]
                for m in range(NT):
                    mm = pe.matmul(ps[:, cols], part[:, b, m, t * P:(t + 1) * P], mix[:, b, m, cols],
                                   start=(i == 0 and m == 0), stop=(i == 1 and m == NT - 1))
                if i == 1:
                    mm.then_inc(u_done[b], 1)

            def mixed(b, t, cols, ps):
                mixed_part(b, t, cols, ps, 0)
                mixed_part(b, t, cols, ps, 1)

            def u_product(b, k):
                pe.wait_ge(t_tail_ready[b], made(k, H, H))
                for t in range(DT):
                    mixed(b, t, slice(0, N), u_ps[b][t])

            pe.wait_ge(zeros_ready, 1)
            for i in range(WARM):
                pe.matmul(gram[1][3][:, :], zeros[:, 0:P], zeros[:, :], start=True, stop=True)
            pe.wait_ge(xyz_head_ready, 1)
            for r in range(NT):
                gram_part(0, 0, r, 0)
            pe.wait_ge(xyz_tail_ready, 1)
            for r in range(NT):
                gram_part(0, 0, r, 1)
                gram_part(0, 0, r, 2)
            gram_tiles(0, 1)
            gram_tiles(0, 2)
            pe.wait_ge(consts_ready, 3)
            column_norms(0)
            gram_tiles(0, 3)
            gram_tiles(1, 0, [0, 1])
            mirror(0)
            gram_tiles(1, 0, [2])
            pe.wait_ge(norms_copied, 1)
            gram_tiles(1, 0, [3])
            gram_tiles(1, 1)
            gram_tiles(1, 2, [0, 1])
            pe.wait_ge(lower_copied, NT - 1)
            mix_tile(0, 0)
            gram_tiles(1, 2, [2, 3])
            mix_tile(0, 1)
            gram_tiles(1, 3)
            mix_tile(0, 2)
            column_norms(1)
            mirror(1)
            mix_tile(0, 3)
            pe.wait_ge(wt_tail_ready, NW)
            pe.wait_ge(norms_copied, 2)
            t_product(0, FIRST, 0)
            pe.wait_ge(mix_ready, NT)
            t_product(1, FIRST, 0)
            pe.wait_ge(lower_copied, 2 * (NT - 1))
            mix_tile(1, 0)
            pe.wait_ge(t_tail_ready[0], H)
            mixed(0, 0, slice(0, N), u_ps[0][0])
            mix_tile(1, 1)
            mix_tile(1, 2)
            mixed_part(0, 1, slice(0, N), u_ps[0][1], 0)
            mix_tile(1, 3)
            mixed_part(0, 1, slice(0, N), u_ps[0][1], 1)
            pe.wait_ge(mix_ready, 2 * NT)
            u_product(1, FIRST)
            with pe.Fori(0, BLOCKS - 2) as j:
                t_product(0, (j, 1), 1)
                t_product(1, (j, 1), 1)
                u_product(0, (j, 1))
                u_product(1, (j, 1))
            t_product(0, LAST, 1)
            t_product(1, LAST, 1)
            for b in range(B):
                pe.wait_ge(t_tail_ready[b], made(LAST, H, H))
                for piece in PIECES[b]:
                    mixed(b, *piece)


def kernel(x, ctx_4096, fside_BxSxS_0):
    import numpy as np
    import concourse.bacc as bacc
    from concourse.bass_utils import run_bass_kernel_spmd

    nc = bacc.Bacc("TRN2", target_bir_lowering=False, num_devices=1)
    arrays, args = {}, []
    wt = fside_BxSxS_0.transpose(0, 2, 1)
    for name, a in (("x", x), ("ctx", ctx_4096), ("wt", wt)):
        a = np.ascontiguousarray(a)
        arrays[f"{name}_dram"] = a
        args.append(nc.dram_tensor(f"{name}_dram", a.shape, mybir.dt.from_np(a.dtype), kind="ExternalInput").ap())
    args.append(nc.dram_tensor("out_dram", x.shape, FP32, kind="ExternalOutput").ap())
    knn_message_passing(nc, *args)
    r = run_bass_kernel_spmd(nc, [arrays], core_ids=[0])
    return r.results[0]["out_dram"]
```
